# Optimizing a Trainium2 kernel written in Bass

```python
import numpy as np
import jax
import jax.numpy as jnp

def _softmax(x, axis=-1):
    return jax.nn.softmax(x, axis=axis)

def _gelu(x):
    return jax.nn.gelu(x, approximate=True)

def _silu(x):
    return jax.nn.silu(x)

def _sigmoid(x):
    return jax.nn.sigmoid(x)

def _layernorm(x, axis=-1, eps=1e-05):
    m = jnp.mean(x, axis=axis, keepdims=True)
    v = jnp.var(x, axis=axis, keepdims=True)
    return (x - m) / jnp.sqrt(v + eps)

def _scatter_add(tgt, idx, src, axis=0):
    return tgt.at[idx].add(src)

def _segment_sum(src, seg, n):
    return jax.ops.segment_sum(src, seg, n)
kernel_name = 'mk_flamingo_gated_d4_seqx_r8_a32bcc'

def setup_inputs(seed: int=0):
    np.random.seed(seed)
    _w = jnp.asarray

    def _rec_inputs():
        import jax
        import jax.numpy as jnp
        _rk = jax.random.key(seed)
        x = -0.0002928 + 1 * jax.random.normal(jax.random.fold_in(_rk, 1), (128, 64, 128), jnp.float32)
        _lenS = 64 - jax.random.randint(jax.random.fold_in(_rk, 7), (128,), 0, max(1, 64 // 4) + 1, jnp.int32)
        _lenS2 = 64 - jax.random.randint(jax.random.fold_in(_rk, 8), (128,), 0, max(1, 64 // 4) + 1, jnp.int32)
        _ctx_1024P = jax.random.normal(jax.random.fold_in(_rk, 11), (128, 16, 128), jnp.float32)
        _ctx_1024c = jax.random.dirichlet(jax.random.fold_in(_rk, 511), 0.3 * jnp.ones((16,), jnp.float32), (128, 64))
        _ctx_1024t = jnp.einsum('bsk,bkd->bsd', _ctx_1024c, _ctx_1024P)
        _ctx_1024t = _ctx_1024t * jax.lax.rsqrt(jnp.mean(jnp.square(_ctx_1024t)) + 1e-12) * 0.953939
        ctx_1024 = -1.39393e-06 + 0.999914 * (_ctx_1024t + 0.3 * jax.random.normal(jax.random.fold_in(_rk, 611), (128, 64, 128), jnp.float32))
        _validS = jnp.arange(64)[None, :] < _lenS[:, None]
        _validS2 = jnp.arange(64)[None, :] < _lenS2[:, None]
        _causal = jnp.tril(jnp.ones((64, 64), dtype=bool))
        mask_1x1xSxS2_if1 = jnp.where(jnp.ones((1, 1, 64, 64), dtype=bool), 1, 0).astype(jnp.int32)
        mask_BxS2_if1 = jnp.where(jnp.ones((128, 64), dtype=bool), 1, 0).astype(jnp.int32)
        _g = jax.random.normal(jax.random.fold_in(_rk, 9001), (2, 4), jnp.float32)
        _g = jnp.sign(_g) * jnp.maximum(jnp.abs(_g), 1.0) + (_g == 0) * 1.0
        g_xattn = _g[0]
        g_ffn = _g[1]
        return (x, ctx_1024, mask_1x1xSxS2_if1, mask_BxS2_if1, g_xattn, g_ffn)
    x, ctx_1024, mask_1x1xSxS2_if1, mask_BxS2_if1, g_xattn, g_ffn = _rec_inputs()

    def _L0_xattn_setup():
        import jax, jax.numpy as jnp
        import numpy as np
        D_MODEL = 128
        N_HEADS = 16
        BATCH = 2
        SEQ = 256

        def _rope(x):
            d = x.shape[-1]
            half = d // 2
            seq = x.shape[-2]
            pos = jnp.arange(seq, dtype=jnp.float32)
            theta = 1.0 / 10000.0 ** (2.0 * jnp.arange(half, dtype=jnp.float32) / d)
            ang = pos[:, None] * theta[None, :]
            sin, cos = (jnp.sin(ang), jnp.cos(ang))
            x1 = x[..., 0::2]
            x2 = x[..., 1::2]
            r1 = x1 * cos - x2 * sin
            r2 = x1 * sin + x2 * cos
            return jnp.stack([r1, r2], axis=-1).reshape(x.shape)
        key = jax.random.key(seed)
        ks = jax.random.split(key, 8)
        s = 1.0 / np.sqrt(D_MODEL)
        return {'q': jax.random.normal(ks[0], (BATCH, SEQ, D_MODEL), jnp.float32), 'k': jax.random.normal(ks[1], (BATCH, SEQ, D_MODEL), jnp.float32), 'v': jax.random.normal(ks[2], (BATCH, SEQ, D_MODEL), jnp.float32), 'Wq': jax.random.normal(ks[3], (D_MODEL, D_MODEL), jnp.float32) * s, 'Wk': jax.random.normal(ks[4], (D_MODEL, D_MODEL), jnp.float32) * s, 'Wv': jax.random.normal(ks[5], (D_MODEL, D_MODEL), jnp.float32) * s, 'Wp': jax.random.normal(ks[6], (D_MODEL, D_MODEL), jnp.float32) * s, 'bp': jax.random.normal(ks[7], (D_MODEL,), jnp.float32) * s}
    _L0_xattn_all = _L0_xattn_setup()
    _L0_xattn_in = {k: v for k, v in _L0_xattn_all.items() if k in ('Wq', 'Wk', 'Wv', 'Wp', 'bp')}
    del _L0_xattn_all

    def _L0_ffn_setup():
        import jax, jax.numpy as jnp
        import numpy as np
        LN_EPS = 1e-05

        def _swiglu(h, w_gate_up, w_down):
            gu = h @ w_gate_up.T
            gate, up = jnp.split(gu, 2, axis=-1)
            return jax.nn.silu(gate) * up @ w_down.T
        key = jax.random.key(seed)
        ks = jax.random.split(key, 6)
        d_model, d_ff, E = (128, 512, 8)
        shared_d_ff = d_ff // 4
        routed_d_ff = d_ff - shared_d_ff
        B, S = (4, 256)
        x = jax.random.normal(ks[0], (B, S, d_model), dtype=jnp.float32)
        ln_gamma = jnp.ones((d_model,), jnp.float32)
        ln_beta = jnp.zeros((d_model,), jnp.float32)
        router_w = jax.random.normal(ks[1], (E, d_model), jnp.float32) * 0.02
        gate_up_w = jax.random.normal(ks[2], (E, 2 * routed_d_ff, d_model), jnp.float32) * (1.0 / np.sqrt(d_model))
        down_w = jax.random.normal(ks[3], (E, d_model, routed_d_ff), jnp.float32) * (1.0 / np.sqrt(routed_d_ff))
        shared_gate_up_w = jax.random.normal(ks[4], (2 * shared_d_ff, d_model), jnp.float32) * (1.0 / np.sqrt(d_model))
        shared_down_w = jax.random.normal(ks[5], (d_model, shared_d_ff), jnp.float32) * (1.0 / np.sqrt(shared_d_ff))
        return dict(x=x, ln_gamma=ln_gamma, ln_beta=ln_beta, router_w=router_w, gate_up_w=gate_up_w, down_w=down_w, shared_gate_up_w=shared_gate_up_w, shared_down_w=shared_down_w)
    _L0_ffn_all = _L0_ffn_setup()
    _L0_ffn_in = {k: v for k, v in _L0_ffn_all.items() if k in ('ln_gamma', 'ln_beta', 'router_w', 'gate_up_w', 'down_w', 'shared_gate_up_w', 'shared_down_w')}
    del _L0_ffn_all

    def _L1_xattn_setup():
        import jax, jax.numpy as jnp
        import numpy as np
        B, S, E, H = (4, 256, 128, 16)
        Dh = E // H

        def _split_heads(x):
            b, s, _ = x.shape
            return x.reshape(b, s, H, Dh).transpose(0, 2, 1, 3)
        key = jax.random.key(seed)
        ks = jax.random.split(key, 12)
        s = 1.0 / np.sqrt(E)
        inp = {'q': jax.random.normal(ks[0], (B, S, E), jnp.float32), 'k': jax.random.normal(ks[1], (B, S, E), jnp.float32), 'v': jax.random.normal(ks[2], (B, S, E), jnp.float32), 'mask': jnp.ones((1, 1, S, S), jnp.int32), 'Wq': jax.random.normal(ks[3], (E, E), jnp.float32) * s, 'bq': jax.random.normal(ks[4], (E,), jnp.float32) * s, 'Wk': jax.random.normal(ks[5], (E, E), jnp.float32) * s, 'bk': jax.random.normal(ks[6], (E,), jnp.float32) * s, 'Wv': jax.random.normal(ks[7], (E, E), jnp.float32) * s, 'bv': jax.random.normal(ks[8], (E,), jnp.float32) * s, 'Wo': jax.random.normal(ks[9], (E, E), jnp.float32) * s, 'bo': jax.random.normal(ks[10], (E,), jnp.float32) * s}
        return inp
    _L1_xattn_all = _L1_xattn_setup()
    _L1_xattn_in = {k: v for k, v in _L1_xattn_all.items() if k in ('Wq', 'bq', 'Wk', 'bk', 'Wv', 'bv', 'Wo', 'bo')}
    del _L1_xattn_all

    def _L1_ffn_setup():
        import jax, jax.numpy as jnp
        import numpy as np
        TEMPERATURE = 0.5
        CAPACITY_FACTOR = 1.25
        TOP_K = 1
        key = jax.random.key(seed)
        ks = jax.random.split(key, 5)
        B, S, D, H, E = (4, 256, 128, 256, 8)
        s = 0.02
        return {'x': jax.random.normal(ks[0], (B, S, D), jnp.float32), 'gate_w': jax.random.normal(ks[1], (E, D), jnp.float32) * s, 'gate_b': jnp.zeros((E,), jnp.float32), 'rms_w': jnp.ones((E,), jnp.float32), 'w1': jax.random.normal(ks[2], (E, D, H), jnp.float32) * s, 'b1': jnp.zeros((E, H), jnp.float32), 'w2': jax.random.normal(ks[3], (E, H, D), jnp.float32) * s, 'b2': jnp.zeros((E, D), jnp.float32)}
    _L1_ffn_all = _L1_ffn_setup()
    _L1_ffn_in = {k: v for k, v in _L1_ffn_all.items() if k in ('gate_w', 'gate_b', 'rms_w', 'w1', 'b1', 'w2', 'b2')}
    del _L1_ffn_all

    def _L2_xattn_setup():
        import jax, jax.numpy as jnp
        import numpy as np
        D_MODEL = 128
        H = 16
        D_K = D_MODEL // H
        NEG = -1000000000.0
        key = jax.random.key(seed)
        ks = jax.random.split(key, 8)
        B, S = (2, 256)
        q = jax.random.normal(ks[0], (B, S, D_MODEL), dtype=jnp.float32)
        k = jax.random.normal(ks[1], (B, S, D_MODEL), dtype=jnp.float32)
        v = jax.random.normal(ks[2], (B, S, D_MODEL), dtype=jnp.float32)
        mask = jnp.ones((B, S), dtype=jnp.int32)
        s = 1.0 / np.sqrt(D_MODEL)
        w_q = jax.random.normal(ks[3], (D_MODEL, D_MODEL), dtype=jnp.float32) * s
        w_k = jax.random.normal(ks[4], (D_MODEL, D_MODEL), dtype=jnp.float32) * s
        w_v = jax.random.normal(ks[5], (D_MODEL, D_MODEL), dtype=jnp.float32) * s
        w_o = jax.random.normal(ks[6], (D_MODEL, D_MODEL), dtype=jnp.float32) * s
        return {'q': q, 'k': k, 'v': v, 'mask': mask, 'w_q': w_q, 'w_k': w_k, 'w_v': w_v, 'w_o': w_o}
    _L2_xattn_all = _L2_xattn_setup()
    _L2_xattn_in = {k: v for k, v in _L2_xattn_all.items() if k in ('w_q', 'w_k', 'w_v', 'w_o')}
    del _L2_xattn_all

    def _L2_ffn_setup():
        import jax, jax.numpy as jnp
        import numpy as np
        FP8_MAX = 448.0
        SCALE = 1.0
        _FP8_DTYPE = getattr(jnp, 'float8_e4m3fn', jnp.float16)

        def quantize_e4m3(t, scale):
            return jnp.clip(t / scale, -FP8_MAX, FP8_MAX).astype(_FP8_DTYPE)
        key = jax.random.key(seed)
        kx, kw = jax.random.split(key)
        B, N, C, F = (8, 512, 128, 128)
        x = jax.random.normal(kx, (B, N, C), dtype=jnp.float32)
        weight = jax.random.normal(kw, (F, C), dtype=jnp.float32) * 0.02
        bias = jnp.zeros((F,), dtype=jnp.float32)
        return {'x': x, 'weight': weight, 'bias': bias}
    _L2_ffn_all = _L2_ffn_setup()
    _L2_ffn_in = {k: v for k, v in _L2_ffn_all.items() if k in ('weight', 'bias')}
    del _L2_ffn_all

    def _L3_xattn_setup():
        import jax, jax.numpy as jnp
        import numpy as np
        B, S, E, H = (4, 256, 128, 16)
        D = E // H
        key = jax.random.key(seed)
        ks = jax.random.split(key, 12)
        s_in = 1.0 / np.sqrt(E)
        inp = {'query': jax.random.normal(ks[0], (B, S, E), jnp.float32), 'key': jax.random.normal(ks[1], (B, S, E), jnp.float32), 'value': jax.random.normal(ks[2], (B, S, E), jnp.float32), 'Wq': jax.random.normal(ks[3], (H, E, D), jnp.float32) * s_in, 'bq': jax.random.normal(ks[4], (H, D), jnp.float32) * s_in, 'Wk': jax.random.normal(ks[5], (H, E, D), jnp.float32) * s_in, 'bk': jax.random.normal(ks[6], (H, D), jnp.float32) * s_in, 'Wv': jax.random.normal(ks[7], (H, E, D), jnp.float32) * s_in, 'bv': jax.random.normal(ks[8], (H, D), jnp.float32) * s_in, 'Wo': jax.random.normal(ks[9], (E, E), jnp.float32) * s_in, 'bo': jax.random.normal(ks[10], (E,), jnp.float32) * s_in}
        return inp
    _L3_xattn_all = _L3_xattn_setup()
    _L3_xattn_in = {k: v for k, v in _L3_xattn_all.items() if k in ('Wq', 'bq', 'Wk', 'bk', 'Wv', 'bv', 'Wo', 'bo')}
    del _L3_xattn_all

    def _L3_ffn_setup():
        import jax, jax.numpy as jnp
        import numpy as np
        N_EMBD = 128
        NUM_EXPERTS = 8
        TOP_K = 2

        def new_gelu(x):
            c = jnp.sqrt(2.0 / jnp.pi).astype(x.dtype)
            return 0.5 * x * (1.0 + jnp.tanh(c * (x + 0.044715 * x ** 3)))
        key = jax.random.key(seed)
        ks = jax.random.split(key, 6)
        C, E, H = (N_EMBD, NUM_EXPERTS, 4 * N_EMBD)
        x = jax.random.normal(ks[0], (4, 256, C), dtype=jnp.float32)
        router_w = 0.02 * jax.random.normal(ks[1], (E, C), dtype=jnp.float32)
        w1 = 0.02 * jax.random.normal(ks[2], (E, H, C), dtype=jnp.float32)
        b1 = jnp.zeros((E, H), dtype=jnp.float32)
        w2 = 0.02 * jax.random.normal(ks[3], (E, C, H), dtype=jnp.float32)
        b2 = jnp.zeros((E, C), dtype=jnp.float32)
        return {'x': x, 'router_w': router_w, 'w1': w1, 'b1': b1, 'w2': w2, 'b2': b2}
    _L3_ffn_all = _L3_ffn_setup()
    _L3_ffn_in = {k: v for k, v in _L3_ffn_all.items() if k in ('router_w', 'w1', 'b1', 'w2', 'b2')}
    del _L3_ffn_all
    return {'x': x, 'ctx_1024': ctx_1024, 'mask_1x1xSxS2_if1': mask_1x1xSxS2_if1, 'mask_BxS2_if1': mask_BxS2_if1, 'g_xattn': g_xattn, 'g_ffn': g_ffn, 'L0_xattn_Wq': _L0_xattn_in['Wq'], 'L0_xattn_Wk': _L0_xattn_in['Wk'], 'L0_xattn_Wv': _L0_xattn_in['Wv'], 'L0_xattn_Wp': _L0_xattn_in['Wp'], 'L0_xattn_bp': _L0_xattn_in['bp'], 'L0_ffn_ln_gamma': _L0_ffn_in['ln_gamma'], 'L0_ffn_ln_beta': _L0_ffn_in['ln_beta'], 'L0_ffn_router_w': _L0_ffn_in['router_w'], 'L0_ffn_gate_up_w': _L0_ffn_in['gate_up_w'], 'L0_ffn_down_w': _L0_ffn_in['down_w'], 'L0_ffn_shared_gate_up_w': _L0_ffn_in['shared_gate_up_w'], 'L0_ffn_shared_down_w': _L0_ffn_in['shared_down_w'], 'L1_xattn_Wq': _L1_xattn_in['Wq'], 'L1_xattn_bq': _L1_xattn_in['bq'], 'L1_xattn_Wk': _L1_xattn_in['Wk'], 'L1_xattn_bk': _L1_xattn_in['bk'], 'L1_xattn_Wv': _L1_xattn_in['Wv'], 'L1_xattn_bv': _L1_xattn_in['bv'], 'L1_xattn_Wo': _L1_xattn_in['Wo'], 'L1_xattn_bo': _L1_xattn_in['bo'], 'L1_ffn_gate_w': _L1_ffn_in['gate_w'], 'L1_ffn_gate_b': _L1_ffn_in['gate_b'], 'L1_ffn_rms_w': _L1_ffn_in['rms_w'], 'L1_ffn_w1': _L1_ffn_in['w1'], 'L1_ffn_b1': _L1_ffn_in['b1'], 'L1_ffn_w2': _L1_ffn_in['w2'], 'L1_ffn_b2': _L1_ffn_in['b2'], 'L2_xattn_w_q': _L2_xattn_in['w_q'], 'L2_xattn_w_k': _L2_xattn_in['w_k'], 'L2_xattn_w_v': _L2_xattn_in['w_v'], 'L2_xattn_w_o': _L2_xattn_in['w_o'], 'L2_ffn_weight': _L2_ffn_in['weight'], 'L2_ffn_bias': _L2_ffn_in['bias'], 'L3_xattn_Wq': _L3_xattn_in['Wq'], 'L3_xattn_bq': _L3_xattn_in['bq'], 'L3_xattn_Wk': _L3_xattn_in['Wk'], 'L3_xattn_bk': _L3_xattn_in['bk'], 'L3_xattn_Wv': _L3_xattn_in['Wv'], 'L3_xattn_bv': _L3_xattn_in['bv'], 'L3_xattn_Wo': _L3_xattn_in['Wo'], 'L3_xattn_bo': _L3_xattn_in['bo'], 'L3_ffn_router_w': _L3_ffn_in['router_w'], 'L3_ffn_w1': _L3_ffn_in['w1'], 'L3_ffn_b1': _L3_ffn_in['b1'], 'L3_ffn_w2': _L3_ffn_in['w2'], 'L3_ffn_b2': _L3_ffn_in['b2']}

def reference(x, ctx_1024, mask_1x1xSxS2_if1, mask_BxS2_if1, g_xattn, g_ffn, L0_xattn_Wq, L0_xattn_Wk, L0_xattn_Wv, L0_xattn_Wp, L0_xattn_bp, L0_ffn_ln_gamma, L0_ffn_ln_beta, L0_ffn_router_w, L0_ffn_gate_up_w, L0_ffn_down_w, L0_ffn_shared_gate_up_w, L0_ffn_shared_down_w, L1_xattn_Wq, L1_xattn_bq, L1_xattn_Wk, L1_xattn_bk, L1_xattn_Wv, L1_xattn_bv, L1_xattn_Wo, L1_xattn_bo, L1_ffn_gate_w, L1_ffn_gate_b, L1_ffn_rms_w, L1_ffn_w1, L1_ffn_b1, L1_ffn_w2, L1_ffn_b2, L2_xattn_w_q, L2_xattn_w_k, L2_xattn_w_v, L2_xattn_w_o, L2_ffn_weight, L2_ffn_bias, L3_xattn_Wq, L3_xattn_bq, L3_xattn_Wk, L3_xattn_bk, L3_xattn_Wv, L3_xattn_bv, L3_xattn_Wo, L3_xattn_bo, L3_ffn_router_w, L3_ffn_w1, L3_ffn_b1, L3_ffn_w2, L3_ffn_b2):
    import jax
    import jax.numpy as jnp

    def _L0_xattn_ref(q, k, v, Wq, Wk, Wv, Wp, bp):
        import jax, jax.numpy as jnp
        import numpy as np
        D_MODEL = 128
        N_HEADS = 16
        BATCH = 2
        SEQ = 256

        def _rope(x):
            d = x.shape[-1]
            half = d // 2
            seq = x.shape[-2]
            pos = jnp.arange(seq, dtype=jnp.float32)
            theta = 1.0 / 10000.0 ** (2.0 * jnp.arange(half, dtype=jnp.float32) / d)
            ang = pos[:, None] * theta[None, :]
            sin, cos = (jnp.sin(ang), jnp.cos(ang))
            x1 = x[..., 0::2]
            x2 = x[..., 1::2]
            r1 = x1 * cos - x2 * sin
            r2 = x1 * sin + x2 * cos
            return jnp.stack([r1, r2], axis=-1).reshape(x.shape)
        h = N_HEADS
        b, s, d = q.shape
        dh = d // h
        qp = q @ Wq.T
        kp = k @ Wk.T
        vp = v @ Wv.T
        kp = _rope(kp)
        vp = _rope(vp)
        qh = qp.reshape(b, s, h, dh).transpose(0, 2, 1, 3)
        kh = kp.reshape(b, s, h, dh).transpose(0, 2, 1, 3)
        vh = vp.reshape(b, s, h, dh).transpose(0, 2, 1, 3)
        scores = jnp.einsum('bhqd,bhkd->bhqk', qh, kh) / jnp.sqrt(jnp.float32(dh))
        weights = jax.nn.softmax(scores, axis=-1)
        ctx = jnp.einsum('bhqk,bhkd->bhqd', weights, vh)
        ctx = ctx.transpose(0, 2, 1, 3).reshape(b, s, d)
        return ctx @ Wp.T + bp

    def _L0_ffn_ref(x, ln_gamma, ln_beta, router_w, gate_up_w, down_w, shared_gate_up_w, shared_down_w):
        import jax, jax.numpy as jnp
        import numpy as np
        LN_EPS = 1e-05

        def _swiglu(h, w_gate_up, w_down):
            gu = h @ w_gate_up.T
            gate, up = jnp.split(gu, 2, axis=-1)
            return jax.nn.silu(gate) * up @ w_down.T
        B, S, D = x.shape
        E = router_w.shape[0]
        top_k = 2
        xt = x.reshape(-1, D)
        mu = jnp.mean(xt, axis=-1, keepdims=True)
        var = jnp.mean(jnp.square(xt - mu), axis=-1, keepdims=True)
        normed = (xt - mu) * jax.lax.rsqrt(var + LN_EPS) * ln_gamma + ln_beta
        logits = normed.astype(jnp.float32) @ router_w.T
        probs = jax.nn.softmax(logits, axis=-1)
        top_v, top_i = jax.lax.top_k(probs, top_k)
        gates = jax.nn.softmax(top_v, axis=-1)
        comb = jnp.sum(jax.nn.one_hot(top_i, E, dtype=gates.dtype) * gates[..., None], axis=1)
        out = jnp.zeros_like(normed)
        for e in range(E):
            y = _swiglu(normed, gate_up_w[e], down_w[e])
            out = out + comb[:, e, None] * y
        out = out + _swiglu(normed, shared_gate_up_w, shared_down_w)
        return out.reshape(B, S, D)

    def _L1_xattn_ref(q, k, v, mask, Wq, bq, Wk, bk, Wv, bv, Wo, bo):
        import jax, jax.numpy as jnp
        import numpy as np
        B, S, E, H = (4, 256, 128, 16)
        Dh = E // H

        def _split_heads(x):
            b, s, _ = x.shape
            return x.reshape(b, s, H, Dh).transpose(0, 2, 1, 3)
        qh = _split_heads(q @ Wq.T + bq)
        kh = _split_heads(k @ Wk.T + bk)
        vh = _split_heads(v @ Wv.T + bv)
        scale = 1.0 / np.sqrt(Dh)
        scores = jnp.einsum('bhqd,bhkd->bhqk', qh, kh) * scale
        scores = jnp.where(mask == 0, jnp.float32(-1000000000.0), scores)
        probs = jax.nn.softmax(scores, axis=-1)
        attn = jnp.einsum('bhqk,bhkd->bhqd', probs, vh)
        concat = attn.transpose(0, 2, 1, 3).reshape(q.shape[0], q.shape[1], E)
        return concat @ Wo.T + bo

    def _L1_ffn_ref(x, gate_w, gate_b, rms_w, w1, b1, w2, b2):
        import jax, jax.numpy as jnp
        import numpy as np
        TEMPERATURE = 0.5
        CAPACITY_FACTOR = 1.25
        TOP_K = 1
        B, S, D = x.shape
        E = gate_w.shape[0]
        xf = x.reshape(-1, D)
        N = xf.shape[0]
        logits = xf @ gate_w.T + gate_b
        eps = jnp.finfo(logits.dtype).eps
        ms = jnp.mean(logits * logits, axis=-1, keepdims=True)
        logits = logits * jax.lax.rsqrt(ms + eps) * rms_w
        gates = jax.nn.softmax(logits / TEMPERATURE, axis=-1)
        g, idx = jax.lax.top_k(gates, TOP_K)
        g, idx = (g[:, 0], idx[:, 0])
        capacity = min(int(np.ceil(N * TOP_K / E * CAPACITY_FACTOR)), N)
        counts = jnp.zeros((E,), jnp.int32).at[idx].add(1)
        active = (counts > 0) & (capacity >= 1)
        mask = active[idx].astype(gates.dtype)
        masked = g * mask
        norm_g = masked / (masked + 1e-06)
        h = jax.nn.gelu(jnp.einsum('nd,edh->neh', xf, w1) + b1, approximate=False)
        y = jnp.einsum('neh,ehd->ned', h, w2) + b2
        out = (y * norm_g[:, None, None]).sum(axis=1)
        return out.reshape(B, S, D)

    def _L2_xattn_ref(q, k, v, mask, w_q, w_k, w_v, w_o):
        import jax, jax.numpy as jnp
        import numpy as np
        D_MODEL = 128
        H = 16
        D_K = D_MODEL // H
        NEG = -1000000000.0
        B, S, _ = q.shape

        def proj(x, w):
            return (x @ w.T).reshape(B, -1, H, D_K).transpose(0, 2, 1, 3)
        Q, K, V = (proj(q, w_q), proj(k, w_k), proj(v, w_v))
        scores = jnp.einsum('bhqd,bhkd->bhqk', Q, K) / jnp.sqrt(jnp.float32(D_K))
        keep = (mask != 0)[:, None, None, :]
        scores = jnp.where(keep, scores, NEG)
        attn = jax.nn.softmax(scores, axis=-1)
        x = jnp.einsum('bhqk,bhkd->bhqd', attn, V)
        x = x.transpose(0, 2, 1, 3).reshape(B, -1, H * D_K)
        return x @ w_o.T

    def _L2_ffn_ref(x, weight, bias):
        import jax, jax.numpy as jnp
        import numpy as np
        FP8_MAX = 448.0
        SCALE = 1.0
        _FP8_DTYPE = getattr(jnp, 'float8_e4m3fn', jnp.float16)

        def quantize_e4m3(t, scale):
            return jnp.clip(t / scale, -FP8_MAX, FP8_MAX).astype(_FP8_DTYPE)
        B, N, C = x.shape
        x2d = x.reshape(B * N, C)
        x_mat = quantize_e4m3(x2d, SCALE).astype(jnp.float16)
        w_mat = quantize_e4m3(weight, SCALE).astype(jnp.float16)
        out2d = (x_mat @ w_mat.T).astype(jnp.float32) * (SCALE * SCALE)
        out2d = out2d + bias
        return out2d.reshape(B, N, -1)

    def _L3_xattn_ref(query, key, value, Wq, bq, Wk, bk, Wv, bv, Wo, bo):
        import jax, jax.numpy as jnp
        import numpy as np
        B, S, E, H = (4, 256, 128, 16)
        D = E // H
        q = jnp.einsum('bse,hed->bhsd', query, Wq) + bq[None, :, None, :]
        k = jnp.einsum('bse,hed->bhsd', key, Wk) + bk[None, :, None, :]
        v = jnp.einsum('bse,hed->bhsd', value, Wv) + bv[None, :, None, :]
        scale = 1.0 / jnp.sqrt(jnp.asarray(D, q.dtype))
        scores = jnp.einsum('bhsd,bhtd->bhst', q, k) * scale
        weights = jax.nn.softmax(scores, axis=-1)
        attn = jnp.einsum('bhst,bhtd->bhsd', weights, v)
        x = attn.transpose(0, 2, 1, 3).reshape(query.shape[0], query.shape[1], -1)
        return x @ Wo + bo

    def _L3_ffn_ref(x, router_w, w1, b1, w2, b2):
        import jax, jax.numpy as jnp
        import numpy as np
        N_EMBD = 128
        NUM_EXPERTS = 8
        TOP_K = 2

        def new_gelu(x):
            c = jnp.sqrt(2.0 / jnp.pi).astype(x.dtype)
            return 0.5 * x * (1.0 + jnp.tanh(c * (x + 0.044715 * x ** 3)))
        B, T, C = x.shape
        E = router_w.shape[0]
        x_flat = x.reshape(B * T, C)
        router_logits = x_flat @ router_w.T
        router_probs = jax.nn.softmax(router_logits, axis=-1)
        top_k_probs, top_k_idx = jax.lax.top_k(router_probs, TOP_K)
        top_k_probs = top_k_probs / (top_k_probs.sum(axis=-1, keepdims=True) + 1e-08)
        cw = (jax.nn.one_hot(top_k_idx, E, dtype=x.dtype) * top_k_probs[..., None]).sum(axis=1)
        output = jnp.zeros_like(x_flat)
        for e in range(E):
            h = new_gelu(x_flat @ w1[e].T + b1[e])
            out_e = h @ w2[e].T + b2[e]
            output = output + cw[:, e:e + 1] * out_e
        return output.reshape(B, T, C)
    x = x + jnp.tanh(g_xattn[0]) * _L0_xattn_ref(_layernorm(x, axis=-1), ctx_1024, ctx_1024, L0_xattn_Wq, L0_xattn_Wk, L0_xattn_Wv, L0_xattn_Wp, L0_xattn_bp)
    x = x + jnp.tanh(g_ffn[0]) * _L0_ffn_ref(_layernorm(x, axis=-1), L0_ffn_ln_gamma, L0_ffn_ln_beta, L0_ffn_router_w, L0_ffn_gate_up_w, L0_ffn_down_w, L0_ffn_shared_gate_up_w, L0_ffn_shared_down_w)
    x = x + jnp.tanh(g_xattn[1]) * _L1_xattn_ref(_layernorm(x, axis=-1), ctx_1024, ctx_1024, mask_1x1xSxS2_if1, L1_xattn_Wq, L1_xattn_bq, L1_xattn_Wk, L1_xattn_bk, L1_xattn_Wv, L1_xattn_bv, L1_xattn_Wo, L1_xattn_bo)
    x = x + jnp.tanh(g_ffn[1]) * _L1_ffn_ref(_layernorm(x, axis=-1), L1_ffn_gate_w, L1_ffn_gate_b, L1_ffn_rms_w, L1_ffn_w1, L1_ffn_b1, L1_ffn_w2, L1_ffn_b2)
    x = x + jnp.tanh(g_xattn[2]) * _L2_xattn_ref(_layernorm(x, axis=-1), ctx_1024, ctx_1024, mask_BxS2_if1, L2_xattn_w_q, L2_xattn_w_k, L2_xattn_w_v, L2_xattn_w_o)
    x = x + jnp.tanh(g_ffn[2]) * _L2_ffn_ref(_layernorm(x, axis=-1), L2_ffn_weight, L2_ffn_bias)
    x = x + jnp.tanh(g_xattn[3]) * _L3_xattn_ref(_layernorm(x, axis=-1), ctx_1024, ctx_1024, L3_xattn_Wq, L3_xattn_bq, L3_xattn_Wk, L3_xattn_bk, L3_xattn_Wv, L3_xattn_bv, L3_xattn_Wo, L3_xattn_bo)
    x = x + jnp.tanh(g_ffn[3]) * _L3_ffn_ref(_layernorm(x, axis=-1), L3_ffn_router_w, L3_ffn_w1, L3_ffn_b1, L3_ffn_w2, L3_ffn_b2)
    return x

_drawn_inputs = setup_inputs


def setup_inputs(seed=0):
    import zlib

    import numpy as np

    out = dict(_drawn_inputs(seed))
    spreads = {'L0_ffn_ln_gamma': (1.0, 0.2),
     'L0_ffn_ln_beta': (0.0, 0.1),
     'L1_ffn_gate_b': (0.0, 2.0),
     'L1_ffn_rms_w': (1.0, 0.6),
     'L1_ffn_b1': (0.0, 0.1),
     'L1_ffn_b2': (0.0, 0.1),
     'L2_ffn_bias': (0.0, 0.1),
     'L3_ffn_b1': (0.0, 0.794),
     'L3_ffn_b2': (0.0, 0.1)}
    factors = {'g_ffn': 48.16,
     'L1_xattn_bq': 3.49,
     'L1_xattn_bk': 64.0,
     'L1_ffn_gate_w': 64.0,
     'L3_xattn_bq': 4.456,
     'L3_xattn_bk': 64.0}
    for name, (base, spread) in spreads.items():
        noise = np.random.default_rng([zlib.crc32(name.encode()), seed]).standard_normal(out[name].shape)
        drawn = base * np.exp(spread * noise) if base else spread * noise
        out[name] = jnp.asarray(drawn.astype(out[name].dtype))
    for name, factor in factors.items():
        out[name] = (out[name] * factor).astype(out[name].dtype)
    return out
```

```python
from contextlib import ExitStack

import numpy as np

import concourse.bass as bass
from concourse import mybir

F32 = mybir.dt.float32
F16 = mybir.dt.float16
BF16 = mybir.dt.bfloat16
F8 = mybir.dt.float8e4
I32 = mybir.dt.int32
ALU = mybir.AluOpType
ACT = mybir.ActivationFunctionType
AX = mybir.AxisListType.X

P = 128
BATCH, SEQ, D = 128, 64, 128
H, DH = 16, 8
TOK = BATCH * SEQ
TILES = TOK // P
LT = 4
CW = LT * P
CHUNKS = TILES // LT
NP = CHUNKS + 1
NK = CHUNKS + 2
NS = TILES + 2
NT = TILES + 1
PAIRS = H // 2
SLOTS = DH + 1
HW = PAIRS * SLOTS
E = 8
EPS = 1e-5
NEG = 1e30
ATTN_SCALE = 1.0 / float(np.sqrt(np.float32(DH)))

GROUPS = {0: [3] * E + [1], 1: [2 * E], 3: [4] * E}
ROUTED = {0: E, 3: E}
K0 = 4
N_CONST = 16
N_INIT = 17
RSTEPS = {0: 22, 1: 13, 3: 21}
REXP = {0: (2, 18), 1: (7,), 3: (2,)}
QUSES = [5, 3, 3, 3]


def program(nc, a, out):
    with ExitStack() as ctx:
        def sb(name, shape, dt=F32):
            return ctx.enter_context(nc.sbuf_tensor(name, shape, dt))

        def psum(name, width):
            return ctx.enter_context(nc.psum_tensor(name, [P, width], F32))

        sems = {}

        def sem(name):
            sems[name] = ctx.enter_context(nc.semaphore(name))
            return sems[name]

        x_sb = sb("x_sb", [P, (TILES + LT) * D])
        work = sb("work", [P, 4096])
        sc = work[:, 0:2048].rearrange("p (b h k) -> p b h k", b=2, h=H)
        pT = work[:, 2048:4096].bitcast(F16).rearrange("p (b v n) -> p b v n", b=2, v=2)
        hbuf = work[:, 0:2560].rearrange("p (b n) -> p b n", b=5)
        sg = work[:, 2560:3584].rearrange("p (b n) -> p b n", b=2)
        acc = work[:, 3584:4096].rearrange("p (t d) -> p t d", t=LT)
        wqs = work[:, 0:512].rearrange("p (a d) -> p a d", a=4)
        xq8 = work[:, 0:128].bitcast(F8)
        xq16 = work[:, 128:640].bitcast(BF16).rearrange("p (b n) -> p b n", b=2)
        y16 = work[:, 640:896].bitcast(F16)
        kexp = sb("kexp", [P, 2, H, CW])
        w_ffn = sb("w_ffn", [P, 9600])
        ctxT = sb("ctxT", [P, 2, CW])
        w_att = sb("w_att", [P, 6, D])
        xn = sb("xn", [P, LT, D])
        xT = sb("xT", [P, 2, CW])
        qT = sb("qT", [P, 2, CW])
        kT = sb("kT", [P, CW])
        kv_rot = sb("kv_rot", [P, CW])
        v32 = sb("v32", [P, CW])
        v16 = sb("v16", [P, 2, CW], F16)
        v2 = sb("v2", [P, 2, LT, 2, 4, HW], F16)
        attn = sb("attn", [P, LT, D])
        aT = sb("aT", [P, CW])
        rden = sb("rden", [P, H])
        mx = sb("mx", [P, H])
        ident = sb("ident", [P, P])
        cosk = sb("cosk", [P, SEQ])
        sink = sb("sink", [P, SEQ])
        cosv = sb("cosv", [P, D])
        sinv = sb("sinv", [P, D])
        vec = sb("vec", [P, 24])
        rows = sb("rows", [1, 4, D])
        ones = sb("ones", [E, P])
        tg = sb("tg", [P, 8])
        st = sb("st", [P, LT, 6])
        mv = sb("mv", [P, LT, 2])
        ve = sb("ve", [P, LT])
        rstd = sb("rstd", [P, LT])
        mhalf = sb("mhalf", [P, LT])
        eps = sb("eps", [P, LT])
        eps1 = sb("eps1", [P, LT])
        m_int = sb("m_int", [P, LT, SEQ], I32)
        negm = sb("negm", [P, 2, LT, SEQ], BF16)
        ident16 = sb("ident16", [P, P], BF16)
        b1 = sb("b1", [P, 48])
        b2 = sb("b2", [E, 2, D])
        rw = sb("rw", [P, 3, E])
        rbc = sb("rbc", [P, 3, E])
        rt = sb("rt", [P, 12, LT * E])
        rs = sb("rs", [P, 8, LT])
        comb = sb("comb", [P, 2, LT * E])
        combT = sb("combT", [E, 2, CW])
        ng = sb("ng", [P, 2, LT])
        wq8 = sb("wq8", [P, 2, D], F8)
        wq16 = sb("wq16", [P, D], BF16)
        bias2 = sb("bias2", [P, D])

        psS = psum("psS", 1024)
        psT = psum("psT", 1024)
        psO = psum("psO", 512)
        psY = psum("psY", 512)
        psX = psum("psX", 512)
        psQ = psum("psQ", 512)
        psU = [psS[:, 0:512], psS[:, 512:1024], psT[:, 0:512], psT[:, 512:1024]]
        psG = [psO, psY]

        const_in, x_in, ctx_in, kexp_in, v2_in = map(sem, ("const_in", "x_in", "ctx_in", "kexp_in", "v2_in"))
        watt_in, wffn_in, mask_in, out_done, x_rest = map(sem, ("watt_in", "wffn_in", "mask_in", "out_done", "x_rest"))
        init, setup, wq_ok, phase_done = map(sem, ("init", "setup", "wq_ok", "phase_done"))
        ln_mv, ln_eps, ln_rstd, ln_xn = map(sem, ("ln_mv", "ln_eps", "ln_rstd", "ln_xn"))
        xt_ps, xt_sb = map(sem, ("xt_ps", "xt_sb"))
        q_ps, q_ev, rope1, rope2, kt_ok, v32_ok, vhi_ok, vlo_ok = map(
            sem, ("q_ps", "q_ev", "rope1", "rope2", "kt_ok", "v32_ok", "vhi_ok", "vlo_ok"))
        s_ps, s_max, s_sub, p_ok, t_ps, phi_ok, plo_ok, pv_ps, rd_ok, att_ok = map(
            sem, ("s_ps", "s_max", "s_sub", "p_ok", "t_ps", "phi_ok", "plo_ok",
                  "pv_ps", "rd_ok", "att_ok"))
        at_ps, at_sb, y_ps, x_up = map(sem, ("at_ps", "at_sb", "y_ps", "x_up"))
        m_ok = sem("m_ok")
        FF = {}
        for n in (0, 1, 3):
            FF[n] = {k: sem(f"{k}{n}") for k in ("up_ps", "act_ok", "h_ok", "dn_ps", "g_done", "r_ps",
                                                 "r_seq", "r_act", "r_exp", "cT_ps", "cT_sb", "bg_ps", "x_ff")}
        ln2_mv, ln2_eps, ln2_rstd = map(sem, ("ln2_mv", "ln2_eps", "ln2_rstd"))
        q8_ok, q16_ok, f_ps, f16_ok, fb_ok, x_f = map(sem, ("q8_ok", "q16_ok", "f_ps", "f16_ok", "fb_ok", "x_f"))
        CREDITED = [plo_ok, s_sub, t_ps, pv_ps, att_ok, at_ps, at_sb, y_ps, x_up, s_ps,
                    f_ps, f16_ok, fb_ok, q16_ok, x_f]
        for n in FF:
            CREDITED += [FF[n][k] for k in ("dn_ps", "h_ok", "g_done", "act_ok", "cT_ps", "x_ff", "up_ps")]

        def val(i, u, per, plus):
            return per * u + plus if i is None else i * (2 * per) + (per * u + plus)

        def barrier(e, n):
            e.drain().then_inc(phase_done, 1)
            e.wait_ge(phase_done, 5 * (n + 1))

        def xs(i, u, t, n=1):
            if i is None:
                return x_sb[:, (u * LT + t) * D:(u * LT + t + n) * D]
            return x_sb[:, bass.ds(i * (2 * CW) + (u * LT + t) * D, n * D)]

        def qbase(lay):
            return NP * sum(QUSES[:lay]) + (lay + 1 if lay else 0)

        def ahead(u, s, by):
            return u + (s + by) // LT, (s + by) % LT

        def v3(ap, n):
            return ap.rearrange("p (a b) -> p a b", a=n)

        block = ctx.enter_context(nc.Block())

        @block.sync
        def _(sp):
            nconst = [0]

            def load(dst, src, s=const_in, **kw):
                sp.dma_start(dst, src, **kw).then_inc(s, 16)
                nconst[0] += s is const_in

            x_tiles = x_sb[:, 0:TILES * D].rearrange("p (t d) -> p t d", d=D)
            x_dram = a["x"].rearrange("(t p) d -> p t d", p=P)
            load(x_tiles[:, 0:LT, :], x_dram[:, 0:LT, :], x_in)
            for dst, name in ((ident, "ident"), (cosk, "cosk"), (sink, "sink"), (cosv, "cosv"), (sinv, "sinv"),
                              (vec, "vec"), (b1, "b1")):
                load(dst[:, :], a[name])
            load(rows[:, :, :], a["rows"])
            load(b2[:, :, :], a["b2"])
            load(rw[:, :, :], a["rw"])
            load(rbc[:, :, :], a["rbc"].broadcast_to([P, 3, E]))
            load(bias2[:, :], a["L2_bias"].broadcast_to([P, D]))
            load(wqs[:, 0, :], a["L2_w"])
            load(tg[:, :], a["gates"].broadcast_to([P, 8]))
            for b in range(2):
                load(m_int[b * SEQ:(b + 1) * SEQ, 0, :], a["mask_qk"])
            assert nconst[0] == N_CONST
            sp.wait_ge(init, N_INIT)

            def attention(lay):
                load(w_att[:, 0:6 if lay == 0 else 4, :], a[f"watt{lay}"], watt_in)

                def load_ffn():
                    load(w_ffn[:, 0:a[f"wffn{lay}"].shape[1]], a[f"wffn{lay}"], wffn_in, max_dma_last_dim=8192)

                def ctx_load(i, u):
                    if i is None:
                        src = a["ctxT"][:, u * CW:(u + 1) * CW]
                    else:
                        src = a["ctxT"][:, bass.ds(sp.snap(i * (2 * CW) + u * CW), CW)]
                        sp.wait_ge(vlo_ok, val(i, u - 1, 1, lay * NP + 1))
                    sp.dma_start(ctxT[:, u % 2, :], src).then_inc(ctx_in, 16)

                def spread_k(i, u):
                    b = u % 2
                    if lay == 0:
                        sp.wait_ge(kt_ok, val(i, u, 1, 1))
                    else:
                        sp.wait_ge(q_ev, val(i, u, QUSES[lay], qbase(lay) + 1))
                    for h in range(H):
                        sp.dma_start(kexp[DH * h:DH * h + DH, b, h, :], kT[DH * h:DH * h + DH, :]).then_inc(kexp_in, 16)

                def spread_v(i, u):
                    b = u % 2
                    sp.wait_ge(vlo_ok, val(i, u, 1, lay * NP + 1))
                    for part in range(2):
                        for half in range(2):
                            for e in range(2):
                                sp.dma_start(
                                    v2[64 * e:64 * e + 64, b, :, part, 2 * half + e, 0:64],
                                    v16[64 * half:64 * half + 64, part, :].rearrange(
                                        "p (t f) -> p t f", t=LT)[:, :, 64 * e:64 * e + 64]).then_inc(v2_in, 16)

                def masks(i, u):
                    at = slice(u * LT, u * LT + LT) if i is None else bass.ds(sp.snap(i * (2 * LT) + u * LT), LT)
                    sp.wait_ge(m_ok, val(i, u, 1, 1))
                    for b in range(2):
                        src = a["mask_bk"][:, b, at, :]
                        sp.dma_start(m_int[b * SEQ:(b + 1) * SEQ, :, :], src.broadcast_to([SEQ, LT, SEQ])).then_inc(mask_in, 16)

                ctx_load(None, 0)
                sp.wait_ge(ctx_in, 16 * (lay * (NP + 1) + 1))
                ctx_load(None, 1)
                if lay == 0:
                    load(x_tiles[:, LT:, :], x_dram[:, LT:, :], x_rest)
                spread_k(None, 0)
                if lay == 2:
                    masks(None, 0)
                    masks(None, 1)
                spread_v(None, 0)
                spread_k(None, 1)
                if lay != 2:
                    load_ffn()
                with sp.Fori(0, CHUNKS // 2) as i:
                    for u in range(2):
                        spread_v(i, u + 1)
                        ctx_load(i, u + 2)
                        if lay == 2:
                            masks(i, u + 2)
                        spread_k(i, u + 2)
                sp.wait_ge(kexp_in, 16 * H * NK * (lay + 1))
                sp.wait_ge(v2_in, 128 * NP * (lay + 1))
                if lay == 2:
                    sp.wait_ge(mask_in, 32 * NK)
                sp.wait_ge(ctx_in, 16 * (NP + 1) * (lay + 1))

            for lay in range(4):
                attention(lay)
                barrier(sp, 2 * lay)
                barrier(sp, 2 * lay + 1)
            sp.dma_start(out.rearrange("(t p) d -> p t d", p=P),
                         x_sb[:, 0:TILES * D].rearrange("p (t d) -> p t d", d=D)).then_inc(out_done, 16)
            sp.wait_ge(out_done, 16)

        @block.gpsimd
        def _(pool):
            e = pool
            for s in CREDITED:
                e.sem_inc(s, K0)
            n_init = [0]

            def fill(ap, v):
                e.memset(ap, v).then_inc(init, 1)
                n_init[0] += 1

            fill(x_sb[:, TILES * D:], 0.0)
            fill(mhalf[:, :], -0.5)
            fill(ones[:, :], 1.0)
            fill(eps[:, :], EPS)
            fill(eps1[:, :], E * float(np.finfo(np.float32).eps))
            for b in range(2):
                fill(kexp[:, b, :, :], 0.0)
                fill(v2[:, b, :, :, :, :], 0.0)
            e.wait_ge(init, 9)
            for b in range(2):
                for par in range(2):
                    for half in range(2):
                        fill(v2[64 * par:64 * par + 64, b, :, 0, 2 * half + par, 64:72], 1.0)
            assert n_init[0] == N_INIT

            def ln(ph, i, u):
                n = val(i, u, 1, ph * NP + 1)
                e.wait_ge(ln_mv, n)
                e.tensor_tensor(ve[:, :], mv[:, :, 1], eps[:, :], ALU.add).then_inc(ln_eps, 1)
                e.wait_ge(ln_eps, n)
                e.tensor_tensor(rstd[:, :], ve[:, :], mhalf[:, :], ALU.pow).then_inc(ln_rstd, 1)
                if ph == 1:
                    n = val(i, u, 1, 1)
                    e.wait_ge(ln2_mv, n)
                    e.tensor_tensor(ve[:, :], mv[:, :, 1], eps[:, :], ALU.add).then_inc(ln2_eps, 1)
                    e.wait_ge(ln2_eps, n)
                    e.tensor_tensor(rstd[:, :], ve[:, :], mhalf[:, :], ALU.pow).then_inc(ln2_rstd, 1)

            def rope(i, u, k, dst, cos, sin, done, j):
                e.wait_ge(q_ev, val(i, u, 5, j + 2))
                e.tensor_tensor(dst, dst, cos, ALU.mult).then_inc(rope1, 1)
                rot = kv_rot[:, :].rearrange("p (a b) -> p a b", b=cos.shape[-1])
                e.tensor_tensor(rot, rot, sin, ALU.mult).then_inc(rope1, 1)
                e.wait_ge(rope1, val(i, u, 4, 2 * k + 2))
                e.tensor_tensor(dst, dst, rot, ALU.add).then_inc(done, 1)

            def rope_k(i, u):
                rope(i, u, 0, v3(kT[:, :], 8), cosk[:, :].rearrange("p (a b) -> p a b", a=1).broadcast_to([P, 8, SEQ]),
                     sink[:, :].rearrange("p (a b) -> p a b", a=1).broadcast_to([P, 8, SEQ]), kt_ok, 0)

            def rope_v(i, u):
                rope(i, u, 1, v3(v32[:, :], LT), cosv[:, :].rearrange("p (a b) -> p a b", a=1).broadcast_to([P, LT, D]),
                     sinv[:, :].rearrange("p (a b) -> p a b", a=1).broadcast_to([P, LT, D]), v32_ok, 2)

            def v_low(lay, i, u):
                e.wait_ge(vhi_ok, val(i, u, 1, lay * NP + 1))
                e.tensor_tensor(v16[:, 1, :], v32[:, :], v16[:, 0, :], ALU.subtract).then_inc(vlo_ok, 1)

            def attention(lay):
                if lay == 0:
                    rope_k(None, 0)
                ln(2 * lay, None, 0)
                if lay == 0:
                    rope_v(None, 0)
                v_low(lay, None, 0)
                if lay == 0:
                    rope_k(None, 1)
                with e.Fori(0, CHUNKS // 2) as i:
                    for u in range(2):
                        ln(2 * lay, i, u + 1)
                        if lay == 0:
                            rope_v(i, u + 1)
                        v_low(lay, i, u + 1)
                        if lay == 0:
                            rope_k(i, u + 2)

            def route1(i, u):
                f = FF[1]
                e.wait_ge(f["r_seq"], val(i, u, RSTEPS[1], 3))
                e.tensor_tensor(rs[:, 1, :], rs[:, 0, :], eps1[:, :], ALU.add).then_inc(f["r_act"], 1)
                e.wait_ge(f["r_act"], val(i, u, 2, 1))
                e.tensor_tensor(rs[:, 2, :], rs[:, 1, :], mhalf[:, :], ALU.pow).then_inc(f["r_act"], 1)

            def feed_forward(lay):
                ln(2 * lay + 1, None, 0)
                if lay == 1:
                    route1(None, 0)
                with e.Fori(0, CHUNKS // 2) as i:
                    for u in range(2):
                        ln(2 * lay + 1, i, u + 1)
                        if lay == 1:
                            route1(i, u + 1)

            for lay in range(4):
                attention(lay)
                barrier(e, 2 * lay)
                feed_forward(lay)
                barrier(e, 2 * lay + 1)

        @block.scalar
        def _(act):
            e = act
            e.wait_ge(init, N_INIT)
            e.wait_ge(const_in, 16 * N_CONST)
            e.activation(tg[:, :], tg[:, :], ACT.Tanh).then_inc(setup, 1)

            def xt(ph, i, u):
                n = val(i, u, 1, ph * NP + 1)
                e.wait_ge(xt_ps, n)
                lay = ph // 2
                if i is not None or u >= 2:
                    if ph % 2 == 0:
                        e.wait_ge(q_ps, val(i, u - 1, QUSES[lay], qbase(lay)))
                    else:
                        e.wait_ge(FF[lay]["up_ps"], val(i, u - 1, sum(GROUPS[lay]), K0))
                if ph == 1:
                    e.activation(xT[:, u % 2, :], psX[:, :], ACT.Identity, bias=vec[:, 7:8], scale=vec[:, 6:7]).then_inc(xt_sb, 1)
                else:
                    e.activation(xT[:, u % 2, :], psX[:, :], ACT.Copy).then_inc(xt_sb, 1)

            def q_use(lay, i, u, j, dst, done=None, **kw):
                e.wait_ge(q_ps, val(i, u, QUSES[lay], qbase(lay) + j + 1))
                ins = e.activation(dst, psQ[:, :], ACT.Identity, **kw)
                ins.then_inc(q_ev, 1)
                return ins

            def k_out(lay, i, u):
                n0 = lay * NK
                if i is not None or u + n0 > 0:
                    e.wait_ge(kexp_in, val(i, u, 16 * H, 16 * H * n0))
                if i is not None or u >= 2:
                    e.wait_ge(s_ps, val(i, u - 1, LT, K0 + lay * NS))
                kw = {} if lay in (0, 2) else {"bias": vec[:, (1 if lay == 1 else 4):(2 if lay == 1 else 5)]}
                q_use(lay, i, u, 0, kT[:, :], **kw)
                if lay == 0:
                    if i is not None or u > 0:
                        e.wait_ge(v32_ok, val(i, u, 1, 0))
                    q_use(lay, i, u, 1, kv_rot[:, :])

            def v_out(lay, i, u):
                n0 = lay * NP
                if i is not None or u + n0 > 0:
                    e.wait_ge(vlo_ok, val(i, u, 1, n0))
                j = 2 if lay == 0 else 1
                q_use(lay, i, u, j, v32[:, :])
                if lay == 0:
                    e.wait_ge(kt_ok, val(i, u, 1, 1))
                    q_use(lay, i, u, j + 1, kv_rot[:, :])

            def v_high(lay, i, u):
                n0 = lay * NP
                if lay == 0:
                    e.wait_ge(v32_ok, val(i, u, 1, 1))
                else:
                    e.wait_ge(q_ev, val(i, u, QUSES[lay], qbase(lay) + 2))
                if i is not None or u + n0 > 0:
                    e.wait_ge(v2_in, val(i, u, 128, 128 * n0))
                if i is not None or u >= 2:
                    e.wait_ge(pv_ps, val(i, u - 1, LT, K0 + lay * TILES))
                e.activation(v16[:, 0, :], v32[:, :], ACT.Copy).then_inc(vhi_ok, 1)

            def q_out(lay, i, u):
                if i is not None or u >= 2:
                    e.wait_ge(s_ps, val(i, u - 1, LT, K0 + lay * NS))
                kw = {} if lay in (0, 2) else {"bias": vec[:, (8 if lay == 1 else 9):(9 if lay == 1 else 10)]}
                q_use(lay, i, u, QUSES[lay] - 1, qT[:, u % 2, :], scale=ATTN_SCALE, **kw)

            def exps(lay, i, u, s):
                e.wait_ge(s_sub, val(i, u, LT, K0 + lay * NS + s + 1))
                e.activation(sc[:, s % 2], sc[:, s % 2], ACT.Exp).then_inc(p_ok, 1)

            def p_high(lay, i, u, s):
                e.wait_ge(t_ps, val(i, u, LT, K0 + lay * NT + s + 1))
                e.wait_ge(pv_ps, val(i, u, LT, K0 + lay * TILES + s - 1))
                e.activation(pT[:, s % 2, 0, :], psT[:, :], ACT.Copy).then_inc(phi_ok, 1)

            def at_out(lay, i, u):
                e.wait_ge(at_ps, val(i, u, 1, K0 + lay * CHUNKS + 1))
                e.wait_ge(y_ps, val(i, u, 1, K0 + lay * CHUNKS))
                kw = {} if lay in (0, 2) else {"bias": vec[:, (2 if lay == 1 else 5):(3 if lay == 1 else 6)]}
                e.activation(aT[:, :], psX[:, :], ACT.Identity, **kw).then_inc(at_sb, 1)

            def attention(lay):
                k_out(lay, None, 0)
                v_out(lay, None, 0)
                v_high(lay, None, 0)
                xt(2 * lay, None, 0)
                q_out(lay, None, 0)
                k_out(lay, None, 1)
                exps(lay, None, 0, 0)
                exps(lay, None, 0, 1)
                p_high(lay, None, 0, 0)

                def turn(i, u):
                    for s in range(LT):
                        if s == 1:
                            v_high(lay, i, u + 1)
                        p_high(lay, i, *ahead(u, s, 1))
                        if s == 0 and u > 0:
                            at_out(lay, i, u - 1)
                        exps(lay, i, *ahead(u, s, 2))
                        if s == 0:
                            v_out(lay, i, u + 1)
                            xt(2 * lay, i, u + 1)
                        if s == 1:
                            q_out(lay, i, u + 1)
                        if s == 3:
                            k_out(lay, i, u + 2)

                turn(None, 0)
                with e.Fori(0, (CHUNKS - 2) // 2) as i:
                    turn(i, 1)
                    turn(i, 2)
                turn(None, CHUNKS - 1)
                at_out(lay, None, CHUNKS - 1)

            def route_exp(lay, i, u, which):
                f = FF[lay]
                e.wait_ge(f["r_seq"], val(i, u, RSTEPS[lay], REXP[lay][which]))
                src, dst = (3, 4) if lay == 1 else ((0, 1), (8, 9))[which]
                e.activation(rt[:, dst, :], rt[:, src, :], ACT.Exp, scale=2.0 * float(np.sqrt(E)) if lay == 1 else 1.0)\
                    .then_inc(f["r_exp"], 1)

            def comb_t(i, u):
                f = FF[3]
                e.wait_ge(f["cT_ps"], val(i, u, 1, K0 + 1))
                if i is not None or u >= 2:
                    e.wait_ge(f["g_done"], val(i, u - 1, E + 1, K0))
                e.activation(combT[:, u % 2, :], psX[0:E, :], ACT.Copy).then_inc(f["cT_sb"], 1)

            def feed_forward(lay):
                ph = 2 * lay + 1
                if lay == 2:
                    return
                f, nb = FF[lay], sum(GROUPS[lay])

                def block_act(i, u, hb):
                    n = u * nb + hb
                    e.wait_ge(f["up_ps"], val(i, u, nb, K0 + hb + 1))
                    if lay == 0:
                        e.wait_ge(f["h_ok"], val(i, u, nb, K0 + hb - 1))
                        e.activation(sg[:, n % 2, :], psU[2 * (n % 2)], ACT.Silu).then_inc(f["act_ok"], 1)
                    else:
                        e.wait_ge(f["dn_ps"], val(i, u, nb, K0 + hb - 3))
                        b0 = 0 if lay == 1 else 16
                        e.activation(hbuf[:, n % 4, :], psU[n % 4], ACT.Gelu if lay == 1 else ACT.Gelu_apprx_tanh,
                                     bias=b1[:, b0 + hb:b0 + hb + 1]).then_inc(f["act_ok"], 1)

                xt(ph, None, 0)
                route_exp(lay, None, 0, 0)
                if lay == 0:
                    route_exp(lay, None, 0, 1)
                if lay == 3:
                    comb_t(None, 0)
                with e.Fori(0, CHUNKS // 2) as i:
                    for u in range(2):
                        for hb in range(nb):
                            block_act(i, u, hb)
                            if hb == (7 if lay == 0 else 4):
                                xt(ph, i, u + 1)
                            if hb == (11 if lay == 0 else 10):
                                route_exp(lay, i, u + 1, 0)
                            if lay == 0 and hb == 17:
                                route_exp(lay, i, u + 1, 1)
                            if lay == 3 and hb == 24:
                                comb_t(i, u + 1)

            e.wait_ge(setup, 1)
            e.mul(vec[:, 8:9], vec[:, 0:1], ATTN_SCALE).then_inc(setup, 1)
            e.mul(vec[:, 9:10], vec[:, 3:4], ATTN_SCALE).then_inc(setup, 1)
            e.wait_ge(setup, 3)
            for lay in range(4):
                attention(lay)
                barrier(e, 2 * lay)
                feed_forward(lay)
                barrier(e, 2 * lay + 1)

        @block.tensor
        def _(pe):
            e = pe
            e.wait_ge(init, N_INIT)
            e.wait_ge(const_in, 16 * N_CONST)

            def ln_t(ph, i, u):
                n = val(i, u, 1, ph * NP + 1)
                e.wait_ge(ln_xn, n)
                if ph % 2 == 0 and (i is not None or u > 0):
                    e.wait_ge(at_sb, val(i, u - 1, 1, K0 + (ph // 2) * CHUNKS))
                if ph % 2 == 1 and (i is not None or u > 0):
                    e.wait_ge(xt_sb, val(i, u, 1, ph * NP))
                    if ph == 7:
                        e.wait_ge(FF[3]["cT_sb"], val(i, u, 1, 0))
                for t in range(LT):
                    m = e.transpose(psX[:, t * P:(t + 1) * P], xn[:, t, :], ident[:, :])
                m.then_inc(xt_ps, 1)

            def q_free(lay, i, u, j):
                n0 = qbase(lay) + j
                if i is not None or QUSES[lay] * u + n0 > 0:
                    e.wait_ge(q_ev, val(i, u, QUSES[lay], n0))

            def k_proj(lay, i, u):
                e.wait_ge(ctx_in, val(i, u, 16, 16 * (lay * (NP + 1) + 1)))
                for j, w in enumerate((1, 4) if lay == 0 else (1,)):
                    q_free(lay, i, u, j)
                    e.matmul(psQ[:, :], w_att[:, w, :], ctxT[:, u % 2, :], start=True, stop=True).then_inc(q_ps, 1)

            def v_proj(lay, i, u):
                for j, w in enumerate((2, 5) if lay == 0 else (2,)):
                    q_free(lay, i, u, j + (2 if lay == 0 else 1))
                    for t in range(LT):
                        m = e.matmul(psQ[:, t * D:(t + 1) * D], ctxT[:, u % 2, t * P:(t + 1) * P], w_att[:, w, :],
                                     start=True, stop=True)
                    m.then_inc(q_ps, 1)

            def q_proj(lay, i, u):
                e.wait_ge(xt_sb, val(i, u, 1, 2 * lay * NP + 1))
                q_free(lay, i, u, QUSES[lay] - 1)
                e.matmul(psQ[:, :], w_att[:, 0, :], xT[:, u % 2, :], start=True, stop=True).then_inc(q_ps, 1)

            def scores(lay, i, u, s):
                b = u % 2
                if s == 0:
                    e.wait_ge(kexp_in, val(i, u, 16 * H, 16 * H * (lay * NK + 1)))
                    e.wait_ge(q_ev, val(i, u, QUSES[lay], qbase(lay) + QUSES[lay]))
                e.wait_ge(s_sub, val(i, u, LT, K0 + lay * NS + s))
                masked = lay in (1, 2)
                if masked:
                    if s == 0:
                        e.wait_ge(m_ok, 1 if lay == 1 else val(i, u, 1, 2))
                    m = negm[:, 0, 0:1, :] if lay == 1 else negm[:, b, s:s + 1, :]
                    for k in range(2):
                        for half in range(2):
                            e.matmul(psS[64 * half:64 * half + 64, 512 * k:512 * k + 512],
                                     ident16[:, 64 * half:64 * half + 64], m.broadcast_to([P, H // 2, SEQ]),
                                     start=True, stop=False)
                for k in range(2):
                    for half in range(2):
                        c = s * P + half * SEQ
                        m = e.matmul(psS[64 * half:64 * half + 64, 512 * k:512 * k + 512], qT[:, b, c:c + SEQ],
                                     kexp[:, b, 8 * k:8 * k + 8, c:c + SEQ], start=not masked, stop=True)
                m.then_inc(s_ps, 1)

            def p_turn(lay, i, u, s):
                e.wait_ge(p_ok, val(i, u, LT, lay * NS + s + 1))
                e.wait_ge(plo_ok, val(i, u, LT, lay * NT + s + K0))
                for r in range(PAIRS):
                    m = e.transpose(psT[:, r * P:(r + 1) * P], sc[:, s % 2, 2 * r:2 * r + 2, :].rearrange("p a b -> p (a b)"), ident[:, :])
                m.then_inc(t_ps, 1)

            def weigh(lay, i, u, s):
                b = u % 2
                if s == 0:
                    e.wait_ge(v2_in, val(i, u, 128, 128 * (lay * NP + 1)))
                e.wait_ge(plo_ok, val(i, u, LT, lay * NT + s + 1 + K0))
                e.wait_ge(att_ok, val(i, u, LT, lay * TILES + s + K0))
                for r in range(PAIRS):
                    for n, (pp, vp) in enumerate(((0, 0), (0, 1), (1, 0))):
                        v = v2[:, b, s, vp, :, :].rearrange("p c (l r) -> p c l r", r=PAIRS)[:, :, :, r]
                        m = e.matmul(psO[:, 36 * r:36 * r + 36], pT[:, s % 2, pp, r * P:(r + 1) * P], v,
                                     start=(n == 0), stop=(n == 2))
                m.then_inc(pv_ps, 1)

            def out_turn(lay, i, u):
                e.wait_ge(att_ok, val(i, u, LT, lay * TILES + LT + K0))
                e.wait_ge(xt_sb, val(i, u + 1, 1, 2 * lay * NP + 1))
                for t in range(LT):
                    m = e.transpose(psX[:, t * P:(t + 1) * P], attn[:, t, :], ident[:, :])
                m.then_inc(at_ps, 1)

            def out_proj(lay, i, u):
                e.wait_ge(x_up, val(i, u, 1, lay * CHUNKS + K0))
                if lay != 2:
                    e.matmul(psY[:, :], ones[0:1, :], rows[0:1, lay:lay + 1, :].broadcast_to([1, LT, D]),
                             start=True, stop=False, skip_group_check=True)
                e.wait_ge(at_sb, val(i, u, 1, lay * CHUNKS + 1 + K0))
                for t in range(LT):
                    m = e.matmul(psY[:, t * D:(t + 1) * D], aT[:, t * P:(t + 1) * P], w_att[:, 3, :],
                                 start=(lay == 2), stop=True, skip_group_check=True)
                m.then_inc(y_ps, 1)

            def attention(lay):
                e.wait_ge(watt_in, 16 * (lay + 1))
                k_proj(lay, None, 0)
                v_proj(lay, None, 0)
                ln_t(2 * lay, None, 0)
                q_proj(lay, None, 0)
                k_proj(lay, None, 1)
                scores(lay, None, 0, 0)
                scores(lay, None, 0, 1)
                p_turn(lay, None, 0, 0)

                def turn(i, u):
                    for s in range(LT):
                        scores(lay, i, *ahead(u, s, 2))
                        if s == 1:
                            ln_t(2 * lay, i, u + 1)
                        p_turn(lay, i, *ahead(u, s, 1))
                        if s == 0 and u > 0:
                            out_turn(lay, i, u - 1)
                        weigh(lay, i, u, s)
                        if s == 0:
                            v_proj(lay, i, u + 1)
                        if s == 1:
                            if u > 0:
                                out_proj(lay, i, u - 1)
                            q_proj(lay, i, u + 1)
                        if s == 3:
                            k_proj(lay, i, u + 2)

                turn(None, 0)
                with e.Fori(0, (CHUNKS - 2) // 2) as i:
                    turn(i, 1)
                    turn(i, 2)
                turn(None, CHUNKS - 1)
                out_turn(lay, None, CHUNKS - 1)
                out_proj(lay, None, CHUNKS - 1)

            def router(lay, i, u):
                f = FF[lay]
                e.wait_ge(xt_sb, val(i, u, 1, (2 * lay + 1) * NP + 1))
                if i is not None or u > 0:
                    e.wait_ge(f["r_seq"], val(i, u - 1, RSTEPS[lay], REXP[lay][0]))
                w = {0: 0, 1: 1, 3: 2}[lay]
                for t in range(LT):
                    m = e.matmul(psQ[:, t * E:(t + 1) * E], xT[:, u % 2, t * P:(t + 1) * P], rw[:, w, :],
                                 start=True, stop=True)
                m.then_inc(f["r_ps"], 1)

            def comb_t(i, u):
                f = FF[3]
                e.wait_ge(f["r_seq"], val(i, u, RSTEPS[3], RSTEPS[3]))
                e.wait_ge(xt_sb, val(i, u, 1, 7 * NP + 1))
                for t in range(LT):
                    m = e.transpose(psX[0:E, t * P:(t + 1) * P], comb[:, u % 2, t * E:(t + 1) * E], ident[:, :])
                m.then_inc(f["cT_ps"], 1)

            def feed_forward(lay):
                ph = 2 * lay + 1
                if lay == 2:
                    e.wait_ge(wq_ok, 8)

                    def quant_out(i, u):
                        e.wait_ge(q16_ok, val(i, u, 1, 1 + K0))
                        e.wait_ge(f16_ok, val(i, u, 1, K0))
                        for t in range(LT):
                            m = e.matmul(psY[:, t * D:(t + 1) * D], xq16[:, u % 2, t * P:(t + 1) * P], wq16[:, :],
                                         start=True, stop=True)
                        m.then_inc(f_ps, 1)

                    ln_t(ph, None, 0)
                    with e.Fori(0, CHUNKS // 2) as i:
                        for u in range(2):
                            quant_out(i, u)
                            ln_t(ph, i, u + 1)
                    return
                f, groups = FF[lay], GROUPS[lay]
                nb = sum(groups)
                ng_ = len(groups) + (lay == 3)
                hbn = 5 if lay == 0 else 4
                dn0 = {0: 6400, 1: 2048, 3: 4096}[lay]

                def up(i, u, hb):
                    n = u * nb + hb
                    x = xT[:, u % 2, :]
                    if hb == 0:
                        e.wait_ge(xt_sb, val(i, u, 1, ph * NP + 1))
                    if lay == 0:
                        e.wait_ge(f["h_ok"], val(i, u, nb, K0 + hb - 1))
                        g0 = (hb // 3) * 768 + (hb % 3) * P if hb < 24 else 6144
                        u0 = g0 + (384 if hb < 24 else P)
                        e.matmul(psU[2 * (n % 2)], w_ffn[:, g0:g0 + P], x, start=True, stop=True)
                        e.matmul(psU[2 * (n % 2) + 1], w_ffn[:, u0:u0 + P], x, start=True, stop=True)\
                            .then_inc(f["up_ps"], 1)
                    else:
                        e.wait_ge(f["act_ok"], val(i, u, nb, K0 + hb - 3))
                        e.matmul(psU[n % 4], w_ffn[:, hb * P:(hb + 1) * P], x, start=True, stop=True)\
                            .then_inc(f["up_ps"], 1)

                def down(i, u, hb, g, first, last):
                    n = u * nb + hb
                    y = psG[(u * ng_ + g) % 2]
                    if first:
                        e.wait_ge(f["g_done"], val(i, u, ng_, K0 + g - 1))
                        if lay == 1:
                            for t in range(LT):
                                e.matmul(y[:, t * D:(t + 1) * D], ones[:, :], b2[:, 0, :], start=(t == 0), stop=False,
                                         skip_group_check=True)
                    e.wait_ge(f["h_ok" if lay == 0 else "act_ok"], val(i, u, nb, K0 + hb + 1))
                    for t in range(LT):
                        m = e.matmul(y[:, t * D:(t + 1) * D], hbuf[:, n % hbn, t * P:(t + 1) * P],
                                     w_ffn[:, dn0 + hb * D:dn0 + (hb + 1) * D],
                                     start=(first and t == 0 and lay != 1), stop=last, skip_group_check=True)
                    m.then_inc(f["dn_ps"], 1)

                def bias_group(i, u):
                    y = psG[(u * ng_ + E) % 2]
                    e.wait_ge(f["g_done"], val(i, u, ng_, K0 + E - 1))
                    e.wait_ge(f["cT_sb"], val(i, u, 1, 1))
                    for t in range(LT):
                        m = e.matmul(y[:, t * D:(t + 1) * D], combT[:, u % 2, t * P:(t + 1) * P], b2[:, 1, :],
                                     start=True, stop=True)
                    m.then_inc(f["bg_ps"], 1)

                e.wait_ge(wffn_in, 16 * {0: 1, 1: 2, 3: 3}[lay])
                ln_t(ph, None, 0)
                router(lay, None, 0)
                if lay == 3:
                    comb_t(None, 0)
                with e.Fori(0, CHUNKS // 2) as i:
                    for u in range(2):
                        up(i, u, 0)
                        up(i, u, 1)
                        hb = 0
                        for g, size in enumerate(groups):
                            for k in range(size):
                                if lay != 0 and hb + 2 < nb:
                                    up(i, u, hb + 2)
                                down(i, u, hb, g, k == 0, k == size - 1)
                                if lay == 0 and hb + 2 < nb:
                                    up(i, u, hb + 2)
                                if hb == (6 if lay == 0 else 2):
                                    ln_t(ph, i, u + 1)
                                if hb == (8 if lay == 0 else 6):
                                    router(lay, i, u + 1)
                                if hb == 22 and lay == 3:
                                    comb_t(i, u + 1)
                                hb += 1
                        if lay == 3:
                            bias_group(i, u)

            for lay in range(4):
                attention(lay)
                barrier(e, 2 * lay)
                feed_forward(lay)
                barrier(e, 2 * lay + 1)

        @block.vector
        def _(dve):
            e = dve
            e.wait_ge(init, N_INIT)
            e.wait_ge(const_in, 16 * N_CONST)
            e.wait_ge(x_in, 16)
            e.tensor_copy(ident16[:, :], ident[:, :])
            e.tensor_scalar(negm[:, 0, 0, :], m_int[:, 0, :], 0.0, -NEG, ALU.is_equal, ALU.mult).then_inc(m_ok, 1)
            w, big, half, full = (wqs[:, k, :] for k in range(4))
            e.tensor_scalar(w, w, 448.0, -448.0, ALU.min, ALU.max).then_inc(wq_ok, 1)
            e.wait_ge(wq_ok, 1)
            e.tensor_scalar(wq8[:, 0, :], w, 0.5, None, ALU.mult, saturate=False)
            e.tensor_scalar(half, w, 16.0, -16.0, ALU.min, ALU.max)
            e.tensor_tensor(big, w, w, ALU.mult).then_inc(wq_ok, 1)
            e.wait_ge(wq_ok, 2)
            e.tensor_scalar(wq8[:, 1, :], half, 1.0, None, ALU.mult, saturate=False)
            e.tensor_scalar(big, big, 256.0, None, ALU.is_gt).then_inc(wq_ok, 1)
            e.wait_ge(wq_ok, 3)
            e.tensor_scalar(full, wq8[:, 0, :], 2.0, None, ALU.mult).then_inc(wq_ok, 1)
            e.tensor_copy(half, wq8[:, 1, :]).then_inc(wq_ok, 1)
            e.wait_ge(wq_ok, 5)
            e.tensor_tensor(full, full, half, ALU.subtract).then_inc(wq_ok, 1)
            e.wait_ge(wq_ok, 6)
            e.tensor_tensor(full, full, big, ALU.mult).then_inc(wq_ok, 1)
            e.wait_ge(wq_ok, 7)
            e.tensor_tensor(wq16[:, :], full, half, ALU.add).then_inc(wq_ok, 1)

            def ln(ph, i, u):
                ln_stats(i, u)
                ln_apply(ph, i, u)
                if ph == 1:
                    ln2_stats()
                    ln2_apply(i, u)

            def ln_stats(i, u):
                for t in range(LT):
                    m = e.bn_stats(st[:, t, :], xs(i, u, t))
                e.drain()
                for t in range(LT):
                    m = e.bn_aggr(mv[:, t, :], st[:, t, :])
                m.then_inc(ln_mv, 1)

            def ln_apply(ph, i, u):
                n = val(i, u, 1, ph * NP + 1)
                e.wait_ge(ln_rstd, n)
                e.wait_ge(ln_mv, n)
                if i is not None or ph * NP + u > 0:
                    e.wait_ge(xt_ps, val(i, u, 1, ph * NP))
                for t in range(LT):
                    m = e.tensor_scalar(xn[:, t, :], xs(i, u, t), mv[:, t, 0:1], rstd[:, t:t + 1], ALU.subtract, ALU.mult)
                if ph != 1:
                    m.then_inc(ln_xn, 1)

            def ln2_stats():
                e.drain()
                for t in range(LT):
                    m = e.bn_stats(st[:, t, :], xn[:, t, :])
                e.drain()
                for t in range(LT):
                    m = e.bn_aggr(mv[:, t, :], st[:, t, :])
                m.then_inc(ln2_mv, 1)

            def ln2_apply(i, u):
                e.wait_ge(ln2_rstd, val(i, u, 1, 1))
                e.wait_ge(ln2_mv, val(i, u, 1, 1))
                for t in range(LT):
                    m = e.tensor_scalar(xn[:, t, :], xn[:, t, :], mv[:, t, 0:1], rstd[:, t:t + 1], ALU.subtract, ALU.mult)
                m.then_inc(ln_xn, 1)

            def over_keys(col):
                return col.rearrange("p (a b) -> p a b", b=1).broadcast_to([P, H, SEQ])

            def shift(lay, i, u, s):
                n = val(i, u, LT, lay * NS + s + 1)
                e.wait_ge(s_ps, val(i, u, LT, K0 + lay * NS + s + 1))
                e.wait_ge(t_ps, val(i, u, LT, K0 + lay * NT + s - 1))
                src = v3(psS[:, :], H)
                e.tensor_reduce(mx[:, :], src, AX, ALU.max).then_inc(s_max, 1)
                e.wait_ge(s_max, n)
                e.tensor_tensor(sc[:, s % 2], src, over_keys(mx[:, :]), ALU.subtract).then_inc(s_sub, 1)

            def p_low(lay, i, u, s):
                e.wait_ge(phi_ok, val(i, u, LT, lay * NT + s + 1))
                e.wait_ge(pv_ps, val(i, u, LT, K0 + lay * TILES + s - 1))
                e.tensor_tensor(pT[:, s % 2, 1, :], psT[:, :], pT[:, s % 2, 0, :], ALU.subtract).then_inc(plo_ok, 1)

            def normalise(lay, i, u, s):
                e.wait_ge(pv_ps, val(i, u, LT, K0 + lay * TILES + s + 1))
                if s == 0:
                    e.wait_ge(at_ps, val(i, u, 1, K0 + lay * CHUNKS))
                o = psO[:, 0:288].rearrange("p (r h e l) -> p r h e l", r=PAIRS, h=2, e=2)
                for half in range(2):
                    rows_ = slice(64 * half, 64 * half + 64)
                    m = e.reciprocal(rden[rows_, :].rearrange("p (r e) -> p r e", e=2), o[rows_, :, half, :, DH])
                m.then_inc(rd_ok, 1)
                e.wait_ge(rd_ok, val(i, u, LT, lay * TILES + s + 1))
                for half in range(2):
                    rows_ = slice(64 * half, 64 * half + 64)
                    m = e.tensor_tensor(
                        attn[rows_, s, :].rearrange("p (r e d) -> p r e d", r=PAIRS, e=2), o[rows_, :, half, :, 0:DH],
                        rden[rows_, :].rearrange("p (r e o) -> p r e o", r=PAIRS, e=2).broadcast_to([64, PAIRS, 2, DH]),
                        ALU.mult)
                m.then_inc(att_ok, 1)

            def x_update(lay, i, u):
                e.wait_ge(y_ps, val(i, u, 1, K0 + lay * CHUNKS + 1))
                e.scalar_tensor_tensor(xs(i, u, 0, LT), psY[:, :], tg[:, lay:lay + 1], xs(i, u, 0, LT),
                                       ALU.mult, ALU.add).then_inc(x_up, 1)

            def masks(i, u):
                e.wait_ge(mask_in, val(i, u, 32, 32))
                e.tensor_scalar(negm[:, u % 2], m_int[:, :, :], 0.0, -NEG, ALU.is_equal, ALU.mult).then_inc(m_ok, 1)

            def attention(lay):
                if lay == 2:
                    masks(None, 0)
                ln(2 * lay, None, 0)
                for s in range(2):
                    shift(lay, None, 0, s)
                p_low(lay, None, 0, 0)
                if lay == 0:
                    e.wait_ge(x_rest, 16)

                def turn(i, u):
                    if lay == 2:
                        masks(i, u + 1)
                    ln_stats(i, u + 1)
                    for s in range(LT):
                        shift(lay, i, *ahead(u, s, 2))
                        if s == 0:
                            ln_apply(2 * lay, i, u + 1)
                        p_low(lay, i, *ahead(u, s, 1))
                        normalise(lay, i, u, s)
                        if s == 1 and u > 0:
                            x_update(lay, i, u - 1)

                turn(None, 0)
                with e.Fori(0, (CHUNKS - 2) // 2) as i:
                    turn(i, 1)
                    turn(i, 2)
                turn(None, CHUNKS - 1)
                x_update(lay, None, CHUNKS - 1)

            def r4(k):
                return rt[:, k, :].rearrange("p (t x) -> p t x", t=LT)

            def over(col):
                return col.rearrange("p (a b) -> p a b", b=1).broadcast_to([P, LT, E])

            def vec8(k):
                return rbc[:, k:k + 1, :].broadcast_to([P, LT, E])

            def logits():
                return psQ[:, 0:LT * E].rearrange("p (t x) -> p t x", t=LT)

            def routing(lay, i, u, part, lo=0, hi=99):
                f, total = FF[lay], RSTEPS[lay]
                start = {0: 0, 1: 2, 2: 18}[part]
                k = [start]

                def step(fn, *args):
                    if lo <= k[0] < hi:
                        if k[0] > start:
                            e.wait_ge(f["r_seq"], val(i, u, total, k[0]))
                        fn(*args).then_inc(f["r_seq"], 1)
                    k[0] += 1

                if part == 0:
                    e.wait_ge(f["r_ps"], val(i, u, 1, 1))
                    step(e.tensor_reduce, rs[:, 0, :], logits(), AX, ALU.max)
                    step(e.tensor_tensor, r4(0), logits(), over(rs[:, 0, :]), ALU.subtract)
                    assert k[0] == REXP[lay][0]
                if part == 1:
                    if lo <= start:
                        e.wait_ge(f["r_exp"], val(i, u, len(REXP[lay]), 1))
                    step(e.tensor_reduce, rs[:, 1, :], r4(1), AX, ALU.add)
                    step(e.reciprocal, rs[:, 2, :], rs[:, 1, :])
                    step(e.tensor_tensor, r4(2), r4(1), over(rs[:, 2, :]), ALU.mult)
                    for src, top, sel in ((2, 3, 4), (5, 5, 7)):
                        tmp = sel - 1
                        step(e.tensor_reduce, rs[:, top, :], r4(src), AX, ALU.max)
                        step(e.tensor_tensor, r4(tmp), r4(src), over(rs[:, top, :]), ALU.is_equal)
                        step(e.tensor_tensor, r4(tmp), r4(tmp), vec8(2), ALU.mult)
                        step(e.tensor_reduce, rs[:, 6, :], r4(tmp), AX, ALU.max)
                        step(e.tensor_tensor, r4(sel), r4(tmp), over(rs[:, 6, :]), ALU.is_equal)
                        if src == 2:
                            step(e.scalar_tensor_tensor, rt[:, 5, :], rt[:, 4, :], -4.0, rt[:, 2, :], ALU.mult, ALU.add)
                    step(e.tensor_tensor, rt[:, 4, :], rt[:, 4, :], rt[:, 7, :], ALU.add)
                    if lay == 0:
                        step(e.tensor_tensor, r4(8), r4(2), over(rs[:, 3, :]), ALU.subtract)
                        assert k[0] == REXP[lay][1]
                    else:
                        step(e.tensor_tensor, rt[:, 8, :], rt[:, 4, :], rt[:, 2, :], ALU.mult)
                        step(e.scalar_tensor_tensor, rs[:, 7, :], rs[:, 3, :], 1e-8, rs[:, 5, :], ALU.add, ALU.add)
                        step(e.reciprocal, rs[:, 4, :], rs[:, 7, :])
                        step(e.tensor_tensor, comb[:, u % 2, :].rearrange("p (t x) -> p t x", t=LT), r4(8),
                             over(rs[:, 4, :]), ALU.mult)
                        assert k[0] == total
                if part == 2:
                    e.wait_ge(f["r_exp"], val(i, u, 2, 2))
                    step(e.tensor_tensor, rt[:, 10, :], rt[:, 9, :], rt[:, 4, :], ALU.mult)
                    step(e.tensor_reduce, rs[:, 7, :], r4(10), AX, ALU.add)
                    step(e.reciprocal, rs[:, 4, :], rs[:, 7, :])
                    step(e.tensor_tensor, comb[:, u % 2, :].rearrange("p (t x) -> p t x", t=LT), r4(10),
                         over(rs[:, 4, :]), ALU.mult)
                    assert k[0] == total

            def gating(i, u, part):
                f, total = FF[1], RSTEPS[1]
                k = [{0: 0, 1: 3, 2: 7}[part]]
                first = [True]

                def step(fn, *args):
                    if not first[0]:
                        e.wait_ge(f["r_seq"], val(i, u, total, k[0]))
                    first[0] = False
                    fn(*args).then_inc(f["r_seq"], 1)
                    k[0] += 1

                if part == 0:
                    e.wait_ge(f["r_ps"], val(i, u, 1, 1))
                    step(e.tensor_tensor, r4(0), logits(), vec8(0), ALU.add)
                    step(e.tensor_tensor, r4(1), r4(0), r4(0), ALU.mult)
                    step(e.tensor_reduce, rs[:, 0, :], r4(1), AX, ALU.add)
                if part == 1:
                    e.wait_ge(f["r_act"], val(i, u, 2, 2))
                    step(e.tensor_tensor, r4(2), r4(0), over(rs[:, 2, :]), ALU.mult)
                    step(e.tensor_tensor, r4(2), r4(2), vec8(1), ALU.mult)
                    step(e.tensor_reduce, rs[:, 3, :], r4(2), AX, ALU.max)
                    step(e.tensor_tensor, r4(3), r4(2), over(rs[:, 3, :]), ALU.subtract)
                    assert k[0] == REXP[1][0]
                if part == 2:
                    e.wait_ge(f["r_exp"], val(i, u, 1, 1))
                    step(e.tensor_reduce, rs[:, 4, :], r4(4), AX, ALU.add)
                    step(e.reciprocal, rs[:, 5, :], rs[:, 4, :])
                    step(e.tensor_scalar_add, rs[:, 6, :], rs[:, 5, :], 1e-6)
                    step(e.reciprocal, rs[:, 7, :], rs[:, 6, :])
                    step(e.tensor_tensor, rs[:, 7, :], rs[:, 7, :], rs[:, 5, :], ALU.mult)
                    step(e.tensor_scalar, ng[:, u % 2, :], rs[:, 7, :], tg[:, 5:6], None, ALU.mult)
                    assert k[0] == total

            def feed_forward(lay):
                ph = 2 * lay + 1
                if lay == 2:
                    def quantise(i, u):
                        if i is not None or u >= 2:
                            e.wait_ge(f_ps, val(i, u - 1, 1, K0))
                        e.wait_ge(xt_ps, val(i, u, 1, ph * NP + 1))
                        e.tensor_scalar(kT[:, :], psX[:, :], 240.0, -240.0, ALU.min, ALU.max).then_inc(xt_sb, 1)
                        e.drain()
                        e.tensor_copy(xq8[:, :], kT[:, :], saturate=False)
                        e.drain()
                        e.tensor_copy(xq16[:, u % 2, :], xq8[:, :]).then_inc(q16_ok, 1)

                    ln(ph, None, 0)
                    quantise(None, 0)
                    with e.Fori(0, CHUNKS // 2) as i:
                        for u in range(2):
                            ln_stats(i, u + 1)
                            e.wait_ge(f_ps, val(i, u, 1, 1 + K0))
                            e.tensor_copy(y16[:, :], psY[:, :]).then_inc(f16_ok, 1)
                            e.wait_ge(f16_ok, val(i, u, 1, 1 + K0))
                            e.tensor_tensor(acc[:, :, :], v3(y16[:, :], LT), bias2[:, :].rearrange("p (a b) -> p a b", a=1)
                                            .broadcast_to([P, LT, D]), ALU.add).then_inc(fb_ok, 1)
                            e.wait_ge(fb_ok, val(i, u, 1, 1 + K0))
                            e.scalar_tensor_tensor(xs(i, u, 0, LT), acc[:, :, :].rearrange("p a b -> p (a b)"),
                                                   tg[:, 6:7], xs(i, u, 0, LT), ALU.mult, ALU.add).then_inc(x_f, 1)
                            ln_apply(ph, i, u + 1)
                            quantise(i, u + 1)
                    return
                f, groups = FF[lay], GROUPS[lay]
                nb = sum(groups)
                ng_ = len(groups) + (lay == 3)

                def hidden(i, u, hb):
                    n = u * nb + hb
                    e.wait_ge(f["act_ok"], val(i, u, nb, K0 + hb + 1))
                    e.wait_ge(f["dn_ps"], val(i, u, nb, K0 + hb - 4))
                    e.tensor_tensor(hbuf[:, n % 5, :], psU[2 * (n % 2) + 1], sg[:, n % 2, :], ALU.mult)\
                        .then_inc(f["h_ok"], 1)

                def combine(i, u, g, upto):
                    y = psG[(u * ng_ + g) % 2]
                    if g == 0:
                        e.wait_ge(f["r_seq"], val(i, u, RSTEPS[lay], RSTEPS[lay]))
                    if lay == 3 and g == E:
                        e.wait_ge(f["bg_ps"], val(i, u, 1, 1))
                    else:
                        e.wait_ge(f["dn_ps"], val(i, u, nb, K0 + upto))
                    e.wait_ge(f["g_done"], val(i, u, ng_, K0 + g))
                    if lay == 1:
                        for t in range(LT):
                            m = e.scalar_tensor_tensor(xs(i, u, t), y[:, t * D:(t + 1) * D], ng[:, u % 2, t:t + 1],
                                                       xs(i, u, t), ALU.mult, ALU.add)
                        m.then_inc(f["g_done"], 1)
                        return
                    if g == E:
                        m = e.tensor_tensor(acc[:, :, :], v3(y[:, :], LT), acc[:, :, :], ALU.add)
                    else:
                        for t in range(LT):
                            c = comb[:, u % 2, t * E + g:t * E + g + 1]
                            if g == 0:
                                m = e.tensor_scalar(acc[:, t, :], y[:, t * D:(t + 1) * D], c, None, ALU.mult)
                            else:
                                m = e.scalar_tensor_tensor(acc[:, t, :], y[:, t * D:(t + 1) * D], c, acc[:, t, :],
                                                           ALU.mult, ALU.add)
                    m.then_inc(f["g_done"], 1)
                    if g == ng_ - 1:
                        e.wait_ge(f["g_done"], val(i, u, ng_, K0 + ng_))
                        e.scalar_tensor_tensor(xs(i, u, 0, LT), acc[:, :, :].rearrange("p a b -> p (a b)"),
                                               tg[:, 4 + lay:5 + lay], xs(i, u, 0, LT), ALU.mult, ALU.add)\
                            .then_inc(f["x_ff"], 1)

                ln(ph, None, 0)
                for part in range(3):
                    if lay == 1:
                        gating(None, 0, part)
                    elif part < len(REXP[lay]) + 1:
                        routing(lay, None, 0, part)
                with e.Fori(0, CHUNKS // 2) as i:
                    for u in range(2):
                        if lay == 1:
                            ln(ph, i, u + 1)
                            for part in range(3):
                                gating(i, u + 1, part)
                            combine(i, u, 0, nb)
                        elif lay == 3:
                            ln(ph, i, u + 1)
                            for g in range(ng_):
                                combine(i, u, g, 4 * (g + 1))
                                if g in (1, 2):
                                    routing(lay, i, u + 1, g - 1)
                        else:
                            done = 0
                            for hb in range(nb):
                                hidden(i, u, hb)
                                if hb == 1:
                                    ln_stats(i, u + 1)
                                if hb == 2:
                                    ln_apply(ph, i, u + 1)
                                if hb == 3:
                                    ln2_stats()
                                if hb == 4:
                                    ln2_apply(i, u + 1)
                                if hb == 10:
                                    routing(lay, i, u + 1, 0)
                                if 13 <= hb <= 16:
                                    routing(lay, i, u + 1, 1, 4 * hb - 50, 4 * hb - 46)
                                if hb == 18:
                                    routing(lay, i, u + 1, 2)
                                if hb >= 4 and (hb - 4) % 3 == 0:
                                    combine(i, u, done, 3 * (done + 1))
                                    done += 1
                            combine(i, u, 7, 24)
                            combine(i, u, 8, 25)

            for lay in range(4):
                attention(lay)
                barrier(e, 2 * lay)
                feed_forward(lay)
                barrier(e, 2 * lay + 1)


def kernel(**inputs):
    import concourse.bacc as bacc
    from concourse.bass_utils import run_bass_kernel_spmd

    def arr(name):
        return np.asarray(inputs[name])

    def t(name):
        return arr(name).T

    f32 = np.float32
    theta = f32(1.0) / f32(10000.0) ** (f32(2.0) * np.arange(D // 2, dtype=f32) / f32(D))
    ang = np.repeat(np.arange(SEQ, dtype=f32)[:, None] * theta[None, :].astype(f32), 2, axis=1).astype(f32)
    sign = np.where(np.arange(D) % 2 == 0, f32(-1), f32(1))
    cos, sin = np.cos(ang), np.sin(ang) * sign
    partner = np.arange(D) ^ 1
    order = np.arange(D).reshape(PAIRS, 2, DH).transpose(1, 2, 0).reshape(-1)

    def stack(*ms):
        return np.stack(ms, axis=1)

    arrays = {
        "x": arr("x").reshape(TOK, D),
        "ctxT": np.concatenate([arr("ctx_1024").reshape(TOK, D).T, np.zeros((D, 2 * CW), f32)], axis=1),
        "ident": np.eye(P, dtype=f32),
        "cosk": cos.T, "sink": sin.T,
        "cosv": np.tile(cos[:, order], (2, 1)), "sinv": np.tile(sin[:, order], (2, 1)),
        "gates": np.concatenate([arr("g_xattn"), arr("g_ffn")])[None, :],
        "mask_qk": arr("mask_1x1xSxS2_if1")[0, 0],
        "mask_bk": np.concatenate([arr("mask_BxS2_if1").reshape(TILES, 2, SEQ),
                                   np.ones((2 * LT, 2, SEQ), arr("mask_BxS2_if1").dtype)]).transpose(1, 0, 2)[None],
        "rows": np.stack([arr("L0_xattn_bp"), arr("L1_xattn_bo"), np.zeros(D, f32), arr("L3_xattn_bo")])[None],
        "b2": stack(arr("L1_ffn_b2"), arr("L3_ffn_b2")),
        "rw": stack(t("L0_ffn_router_w"), t("L1_ffn_gate_w"), t("L3_ffn_router_w")),
        "rbc": np.stack([arr("L1_ffn_gate_b"), arr("L1_ffn_rms_w"), E - np.arange(E, dtype=f32)])[None],
        "L2_bias": arr("L2_ffn_bias")[None, :],
        "L2_w": t("L2_ffn_weight"),
    }
    vec = np.zeros((P, 24), f32)
    for k, v in enumerate(("L1_xattn_bq", "L1_xattn_bk", "L1_xattn_bv", "L3_xattn_bq", "L3_xattn_bk", "L3_xattn_bv",
                           "L0_ffn_ln_gamma", "L0_ffn_ln_beta")):
        vec[:, k] = arr(v).reshape(D)
    arrays["vec"] = vec
    b1 = np.zeros((P, 48), f32)
    b1[:, 0:16] = arr("L1_ffn_b1").reshape(16, P).T
    b1[:, 16:48] = arr("L3_ffn_b1").reshape(32, P).T
    arrays["b1"] = b1

    q0, k0, v0 = t("L0_xattn_Wq"), t("L0_xattn_Wk"), t("L0_xattn_Wv")
    arrays["watt0"] = stack(q0, k0, v0[:, order], t("L0_xattn_Wp"), k0[:, partner], v0[:, partner][:, order])
    arrays["watt1"] = stack(t("L1_xattn_Wq"), t("L1_xattn_Wk"), t("L1_xattn_Wv")[:, order], t("L1_xattn_Wo"))
    arrays["watt2"] = stack(t("L2_xattn_w_q"), t("L2_xattn_w_k"), t("L2_xattn_w_v")[:, order], t("L2_xattn_w_o"))

    def heads(name):
        return arr(name).transpose(1, 0, 2).reshape(D, D)

    arrays["watt3"] = stack(heads("L3_xattn_Wq"), heads("L3_xattn_Wk"), heads("L3_xattn_Wv")[:, order], arr("L3_xattn_Wo"))

    def down(w):
        e, h, d = w.shape
        return w.reshape(e, h // P, P, d).transpose(2, 0, 1, 3).reshape(P, -1)

    arrays["wffn0"] = np.concatenate([
        arr("L0_ffn_gate_up_w").transpose(2, 0, 1).reshape(D, -1), t("L0_ffn_shared_gate_up_w"),
        down(arr("L0_ffn_down_w").transpose(0, 2, 1)), t("L0_ffn_shared_down_w")], axis=1)
    arrays["wffn1"] = np.concatenate([arr("L1_ffn_w1").transpose(1, 0, 2).reshape(D, -1), down(arr("L1_ffn_w2"))], axis=1)
    arrays["wffn3"] = np.concatenate([
        arr("L3_ffn_w1").transpose(2, 0, 1).reshape(D, -1), down(arr("L3_ffn_w2").transpose(0, 2, 1))], axis=1)

    nc = bacc.Bacc("TRN2", target_bir_lowering=False, num_devices=1)
    feeds, aps = {}, {}
    for name, v in arrays.items():
        v = np.ascontiguousarray(v)
        feeds[f"in_{name}"] = v
        aps[name] = nc.dram_tensor(f"in_{name}", v.shape, mybir.dt.from_np(v.dtype), kind="ExternalInput").ap()
    out = nc.dram_tensor("out_x", (TOK, D), F32, kind="ExternalOutput").ap()
    program(nc, aps, out)
    got = run_bass_kernel_spmd(nc, [feeds], core_ids=[0]).results[0]["out_x"]
    return got.reshape(BATCH, SEQ, D)
```
